# Optimizing a Trainium2 kernel written in Bass

```python
import numpy as np
import jax
import jax.numpy as jnp

def _softmax(x, axis=-1):
    return jax.nn.softmax(x, axis=axis)

def _gelu(x):
    return jax.nn.gelu(x, approximate=True)

def _silu(x):
    return jax.nn.silu(x)

def _sigmoid(x):
    return jax.nn.sigmoid(x)

def _layernorm(x, axis=-1, eps=1e-05):
    m = jnp.mean(x, axis=axis, keepdims=True)
    v = jnp.var(x, axis=axis, keepdims=True)
    return (x - m) / jnp.sqrt(v + eps)

def _scatter_add(tgt, idx, src, axis=0):
    return tgt.at[idx].add(src)

def _segment_sum(src, seg, n):
    return jax.ops.segment_sum(src, seg, n)
kernel_name = 'mk_dlrm_tower_d1_rec_r8_ad517f'

def setup_inputs(seed: int=0):
    np.random.seed(seed)
    _w = jnp.asarray

    def _rec_inputs():
        import jax
        import jax.numpy as jnp
        _tk = jax.random.key(seed)
        ids = jnp.stack([jax.random.randint(jax.random.fold_in(_tk, 200 + f), (512,), 0, v, jnp.int32) for f, v in enumerate([1000, 12500, 1000, 12500, 1000, 1250, 12500, 12500, 125000, 12500, 12500, 12500, 1250, 1000, 1250, 12500, 1000, 1000, 12500, 1250, 1000, 1000, 1000, 1000, 1000, 1000])], axis=1)
        tbl_0 = 0.05 * jax.random.normal(jax.random.fold_in(_tk, 500 + 0), (1000, 128), jnp.float32)
        tbl_1 = 0.05 * jax.random.normal(jax.random.fold_in(_tk, 500 + 1), (12500, 128), jnp.float32)
        tbl_2 = 0.05 * jax.random.normal(jax.random.fold_in(_tk, 500 + 2), (1000, 128), jnp.float32)
        tbl_3 = 0.05 * jax.random.normal(jax.random.fold_in(_tk, 500 + 3), (12500, 128), jnp.float32)
        tbl_4 = 0.05 * jax.random.normal(jax.random.fold_in(_tk, 500 + 4), (1000, 128), jnp.float32)
        tbl_5 = 0.05 * jax.random.normal(jax.random.fold_in(_tk, 500 + 5), (1250, 128), jnp.float32)
        tbl_6 = 0.05 * jax.random.normal(jax.random.fold_in(_tk, 500 + 6), (12500, 128), jnp.float32)
        tbl_7 = 0.05 * jax.random.normal(jax.random.fold_in(_tk, 500 + 7), (12500, 128), jnp.float32)
        tbl_8 = 0.05 * jax.random.normal(jax.random.fold_in(_tk, 500 + 8), (125000, 128), jnp.float32)
        tbl_9 = 0.05 * jax.random.normal(jax.random.fold_in(_tk, 500 + 9), (12500, 128), jnp.float32)
        tbl_10 = 0.05 * jax.random.normal(jax.random.fold_in(_tk, 500 + 10), (12500, 128), jnp.float32)
        tbl_11 = 0.05 * jax.random.normal(jax.random.fold_in(_tk, 500 + 11), (12500, 128), jnp.float32)
        tbl_12 = 0.05 * jax.random.normal(jax.random.fold_in(_tk, 500 + 12), (1250, 128), jnp.float32)
        tbl_13 = 0.05 * jax.random.normal(jax.random.fold_in(_tk, 500 + 13), (1000, 128), jnp.float32)
        tbl_14 = 0.05 * jax.random.normal(jax.random.fold_in(_tk, 500 + 14), (1250, 128), jnp.float32)
        tbl_15 = 0.05 * jax.random.normal(jax.random.fold_in(_tk, 500 + 15), (12500, 128), jnp.float32)
        tbl_16 = 0.05 * jax.random.normal(jax.random.fold_in(_tk, 500 + 16), (1000, 128), jnp.float32)
        tbl_17 = 0.05 * jax.random.normal(jax.random.fold_in(_tk, 500 + 17), (1000, 128), jnp.float32)
        tbl_18 = 0.05 * jax.random.normal(jax.random.fold_in(_tk, 500 + 18), (12500, 128), jnp.float32)
        tbl_19 = 0.05 * jax.random.normal(jax.random.fold_in(_tk, 500 + 19), (1250, 128), jnp.float32)
        tbl_20 = 0.05 * jax.random.normal(jax.random.fold_in(_tk, 500 + 20), (1000, 128), jnp.float32)
        tbl_21 = 0.05 * jax.random.normal(jax.random.fold_in(_tk, 500 + 21), (1000, 128), jnp.float32)
        tbl_22 = 0.05 * jax.random.normal(jax.random.fold_in(_tk, 500 + 22), (1000, 128), jnp.float32)
        tbl_23 = 0.05 * jax.random.normal(jax.random.fold_in(_tk, 500 + 23), (1000, 128), jnp.float32)
        tbl_24 = 0.05 * jax.random.normal(jax.random.fold_in(_tk, 500 + 24), (1000, 128), jnp.float32)
        tbl_25 = 0.05 * jax.random.normal(jax.random.fold_in(_tk, 500 + 25), (1000, 128), jnp.float32)
        _rk = jax.random.fold_in(_tk, 7)
        r_dense_features = -0.000520686 + 1.00062 * jax.random.normal(jax.random.fold_in(_rk, 101), (512, 128), jnp.float32)
        W_top1 = 0.0405887 * jax.random.normal(jax.random.fold_in(_tk, 801), (607, 512), jnp.float32)
        W_top2 = 0.0441942 * jax.random.normal(jax.random.fold_in(_tk, 802), (512, 256), jnp.float32)
        W_top3 = 0.0625 * jax.random.normal(jax.random.fold_in(_tk, 803), (256, 1), jnp.float32)
        b_top1 = jnp.zeros((512,), jnp.float32)
        b_top2 = jnp.zeros((256,), jnp.float32)
        return (r_dense_features, ids, tbl_0, tbl_1, tbl_2, tbl_3, tbl_4, tbl_5, tbl_6, tbl_7, tbl_8, tbl_9, tbl_10, tbl_11, tbl_12, tbl_13, tbl_14, tbl_15, tbl_16, tbl_17, tbl_18, tbl_19, tbl_20, tbl_21, tbl_22, tbl_23, tbl_24, tbl_25, W_top1, b_top1, W_top2, b_top2, W_top3)
    r_dense_features, ids, tbl_0, tbl_1, tbl_2, tbl_3, tbl_4, tbl_5, tbl_6, tbl_7, tbl_8, tbl_9, tbl_10, tbl_11, tbl_12, tbl_13, tbl_14, tbl_15, tbl_16, tbl_17, tbl_18, tbl_19, tbl_20, tbl_21, tbl_22, tbl_23, tbl_24, tbl_25, W_top1, b_top1, W_top2, b_top2, W_top3 = _rec_inputs()

    def _L0_rec_setup():
        import jax, jax.numpy as jnp
        import numpy as np
        NUM_SPARSE = 26
        EMBED_DIM = 128
        BATCH = 2048
        key = jax.random.key(seed)
        k1, k2 = jax.random.split(key)
        dense_features = jax.random.normal(k1, (BATCH, EMBED_DIM), dtype=jnp.float32)
        sparse_features = jax.random.normal(k2, (BATCH, NUM_SPARSE, EMBED_DIM), dtype=jnp.float32)
        return {'dense_features': dense_features, 'sparse_features': sparse_features}
    _L0_rec_all = _L0_rec_setup()
    _L0_rec_in = {k: v for k, v in _L0_rec_all.items() if k in ()}
    del _L0_rec_all
    return {'r_dense_features': r_dense_features, 'ids': ids, 'tbl_0': tbl_0, 'tbl_1': tbl_1, 'tbl_2': tbl_2, 'tbl_3': tbl_3, 'tbl_4': tbl_4, 'tbl_5': tbl_5, 'tbl_6': tbl_6, 'tbl_7': tbl_7, 'tbl_8': tbl_8, 'tbl_9': tbl_9, 'tbl_10': tbl_10, 'tbl_11': tbl_11, 'tbl_12': tbl_12, 'tbl_13': tbl_13, 'tbl_14': tbl_14, 'tbl_15': tbl_15, 'tbl_16': tbl_16, 'tbl_17': tbl_17, 'tbl_18': tbl_18, 'tbl_19': tbl_19, 'tbl_20': tbl_20, 'tbl_21': tbl_21, 'tbl_22': tbl_22, 'tbl_23': tbl_23, 'tbl_24': tbl_24, 'tbl_25': tbl_25, 'W_top1': W_top1, 'b_top1': b_top1, 'W_top2': W_top2, 'b_top2': b_top2, 'W_top3': W_top3}

def reference(r_dense_features, ids, tbl_0, tbl_1, tbl_2, tbl_3, tbl_4, tbl_5, tbl_6, tbl_7, tbl_8, tbl_9, tbl_10, tbl_11, tbl_12, tbl_13, tbl_14, tbl_15, tbl_16, tbl_17, tbl_18, tbl_19, tbl_20, tbl_21, tbl_22, tbl_23, tbl_24, tbl_25, W_top1, b_top1, W_top2, b_top2, W_top3):
    import jax
    import jax.numpy as jnp

    def _L0_rec_ref(dense_features, sparse_features):
        import jax, jax.numpy as jnp
        import numpy as np
        NUM_SPARSE = 26
        EMBED_DIM = 128
        BATCH = 2048
        F = NUM_SPARSE + 1
        combined = jnp.concatenate([dense_features[:, None, :], sparse_features], axis=1)
        interactions = jnp.einsum('bfd,bgd->bfg', combined, combined)
        iu, ju = jnp.triu_indices(F, k=1)
        interactions_flat = interactions[:, iu, ju]
        return jnp.concatenate([dense_features, interactions_flat], axis=1)
    e = jnp.stack([tbl_0[ids[:, 0]], tbl_1[ids[:, 1]], tbl_2[ids[:, 2]], tbl_3[ids[:, 3]], tbl_4[ids[:, 4]], tbl_5[ids[:, 5]], tbl_6[ids[:, 6]], tbl_7[ids[:, 7]], tbl_8[ids[:, 8]], tbl_9[ids[:, 9]], tbl_10[ids[:, 10]], tbl_11[ids[:, 11]], tbl_12[ids[:, 12]], tbl_13[ids[:, 13]], tbl_14[ids[:, 14]], tbl_15[ids[:, 15]], tbl_16[ids[:, 16]], tbl_17[ids[:, 17]], tbl_18[ids[:, 18]], tbl_19[ids[:, 19]], tbl_20[ids[:, 20]], tbl_21[ids[:, 21]], tbl_22[ids[:, 22]], tbl_23[ids[:, 23]], tbl_24[ids[:, 24]], tbl_25[ids[:, 25]]], axis=1)
    z = _L0_rec_ref(r_dense_features, e)
    z = z.reshape(z.shape[0], -1)
    h = jnp.concatenate([z, r_dense_features], axis=1)
    h = jnp.maximum(h @ W_top1 + b_top1, 0.0)
    h = jnp.maximum(h @ W_top2 + b_top2, 0.0)
    y = h @ W_top3
    return y

_drawn_inputs = setup_inputs


def setup_inputs(seed=0):
    import zlib

    import numpy as np

    out = dict(_drawn_inputs(seed))
    spreads = {'b_top1': (0.0, 0.1), 'b_top2': (0.0, 0.1)}
    factors = {}
    for name, (base, spread) in spreads.items():
        noise = np.random.default_rng([zlib.crc32(name.encode()), seed]).standard_normal(out[name].shape)
        drawn = base * np.exp(spread * noise) if base else spread * noise
        out[name] = jnp.asarray(drawn.astype(out[name].dtype))
    for name, factor in factors.items():
        out[name] = (out[name] * factor).astype(out[name].dtype)
    return out
```

```python
from contextlib import ExitStack

import concourse.bass as bass
from concourse import mybir

B = 512
D = 128
NT = 26
F = NT + 1
P = 128
T = B // P
QS = 32
H1, H2 = 512, 256
N1, N2 = H1 // P, H2 // P
GROUP = 4
NG = -(-F // GROUP)
GROUPS = [range(g * GROUP, min(F, (g + 1) * GROUP)) for g in range(NG)]
SHIFTS = (F - 1) // 2
PF = 9
PC = F // PF
KP = PF * SHIFTS
ZG = F + SHIFTS
SLOTS = P // 4


def pair_rows():
    rows = []
    for f in range(F):
        for k in range(1, SHIFTS + 1):
            lo, hi = sorted((f, (f + k) % F))
            rows.append(D + lo * F - lo * (lo + 1) // 2 + hi - lo - 1)
    return rows


def build(nc, dense, ids, tables, w1, b1, w2, b2, w3, eye, out):
    fp32, i32 = mybir.dt.float32, mybir.dt.int32
    ALU = mybir.AluOpType
    ACT = mybir.ActivationFunctionType

    with ExitStack() as ctx:

        def sb(name, shape, dt=fp32):
            return ctx.enter_context(nc.sbuf_tensor(name, shape, dt))

        def pb(name, shape):
            return ctx.enter_context(nc.psum_tensor(name, shape, fp32))

        def sem(name):
            return ctx.enter_context(nc.semaphore(name))

        idx = sb("idx", [P, T, NT], i32)
        rows = sb("rows", [P, T, F, D])
        xt = sb("xt", [D, T, P, F])
        zs = sb("zs", [P, ZG * QS])
        flat = sb("flat", [P, F * SHIFTS])
        pairs = sb("pairs", [KP, PC, P])
        w1s = sb("w1s", [P, 2 + PC, H1])
        w2s = sb("w2s", [P, N1, H2])
        w3s = sb("w3s", [P, N2])
        b1s = sb("b1s", [P, N1])
        b2s = sb("b2s", [P, N2])
        eyes = sb("eyes", [P, P])
        h1 = sb("h1", [P, N1, P])
        h2 = sb("h2", [P, N2, P])
        y = sb("y", [1, B])

        p_tr = [pb(f"p_tr{i}", [P, GROUP * P]) for i in range(2)]
        p_gram = pb("p_gram", [P, SLOTS * QS])
        p_pair = pb("p_pair", [P, 512])
        p_h1 = [pb(f"p_h1{i}", [P, N1 // 2, P]) for i in range(2)]
        p_h2 = pb("p_h2", [P, 512])

        s_ids = sem("s_ids")
        s_dense = sem("s_dense")
        s_eye = sem("s_eye")
        s_w1 = sem("s_w1")
        s_w2 = sem("s_w2")
        s_small = sem("s_small")
        s_rows = [[sem(f"s_rows{t}_{g}") for g in range(NG)] for t in range(T)]
        s_clear = sem("s_clear")
        s_tr = sem("s_tr")
        s_xt_act = sem("s_xt_act")
        s_xt_dve = sem("s_xt_dve")
        s_gram = sem("s_gram")
        s_z = sem("s_z")
        s_flat = sem("s_flat")
        s_pt = sem("s_pt")
        s_pairs = sem("s_pairs")
        s_l1 = sem("s_l1")
        s_h1a = sem("s_h1a")
        s_h1b = sem("s_h1b")
        s_l2 = sem("s_l2")
        s_h2 = sem("s_h2")
        s_l3 = sem("s_l3")
        s_y = sem("s_y")
        s_out = sem("s_out")

        block = ctx.enter_context(nc.Block())

        @block.sync
        def _(sp):
            sp.dma_start(idx[:, :, :], ids.rearrange("(t p) f -> p t f", p=P)).then_inc(s_ids, 16)
            sp.dma_start(rows[:, :, 0, :], dense.rearrange("(t p) d -> p t d", p=P)).then_inc(s_dense, 16)
            sp.dma_start(w1s[:, 0:2, :], w1[0 : 2 * D, :].rearrange("(k p) n -> p k n", p=D)).then_inc(s_w1, 16)
            sp.dma_start(w1s[0:KP, 2 : 2 + PC, :], w1[2 * D :, :].rearrange("(c p) n -> p c n", p=KP)).then_inc(s_w1, 16)
            sp.dma_start(w2s[:, :, :], w2.rearrange("(k p) n -> p k n", p=P)).then_inc(s_w2, 16)
            sp.wait_ge(s_y, T)
            sp.dma_start(out.rearrange("b o -> o b"), y[:, :]).then_inc(s_out, 16)
            sp.wait_ge(s_out, 16)

        @block.gpsimd
        def _(pool):
            pool.wait_ge(s_ids, 16)
            for t in range(T):
                for g, feats in enumerate(GROUPS):
                    for f in feats:
                        if f:
                            pool.indirect_dma_start(
                                rows[:, t, f, :], None, tables[f - 1],
                                bass.IndirectOffsetOnAxis(ap=idx[:, t, f - 1 : f], axis=0),
                            ).then_inc(s_rows[t][g], 16)

        def copy_group(copy, t, g):
            feats = GROUPS[g]
            n = len(feats)
            dst = xt[:, t, :, feats[0] : feats[0] + n].rearrange("d b f -> d f b")
            src = p_tr[(NG * t + g) % 2][:, 0 : n * P].rearrange("d (f b) -> d f b", f=n)
            return copy(dst, src)

        @block.scalar
        def _(act):
            act.dma_start(eyes[:, :], eye).then_inc(s_eye, 16)
            act.dma_start(w3s[:, :], w3).then_inc(s_small, 16)
            act.dma_start(b1s[:, :], b1).then_inc(s_small, 16)
            act.dma_start(b2s[:, :], b2).then_inc(s_small, 16)
            act.wait_ge(s_small, 48)
            for t in range(T):
                for g in range(NG):
                    n = NG * t + g
                    if n % 2 == 0:
                        act.wait_ge(s_tr, n + 1)
                        copy_group(nc.scalar.copy, t, g).then_inc(s_xt_act, 1)
                act.wait_ge(s_z, t + 1)
                if t:
                    act.wait_ge(s_pt, t)
                z = zs[:, :]
                z = bass.AP(z.tensor, z.offset + QS, [z.ap[0], [QS + 1, F], [QS, SHIFTS]])
                nc.scalar.copy(flat[:, :].rearrange("p (f k) -> p f k", f=F), z).then_inc(s_flat, 1)
                act.wait_ge(s_pt, t + 1)
                if t:
                    act.wait_ge(s_l1, 2 * t)
                nc.scalar.copy(pairs[:, :, :], p_pair[0:KP, 0 : PC * P].rearrange("p (c b) -> p c b", c=PC)).then_inc(s_pairs, 1)
                act.wait_ge(s_l1, 2 * t + 1)
                for n in range(N1 // 2):
                    i = nc.scalar.activation(h1[:, n, :], p_h1[0][:, n, :], ACT.Relu, bias=b1s[:, n : n + 1])
                i.then_inc(s_h1a, 1)
                act.wait_ge(s_l2, t + 1)
                for n in range(N2):
                    i = nc.scalar.activation(h2[:, n, :], p_h2[:, n * P : (n + 1) * P], ACT.Relu, bias=b2s[:, n : n + 1])
                i.then_inc(s_h2, 1)

        @block.vector
        def _(dve):
            nc.vector.memset(p_gram[:, :], 0.0).then_inc(s_clear, 1)
            dve.wait_ge(s_small, 48)
            for t in range(T):
                for g in range(NG):
                    n = NG * t + g
                    if n % 2 == 1:
                        dve.wait_ge(s_tr, n + 1)
                        copy_group(nc.vector.tensor_copy, t, g).then_inc(s_xt_dve, 1)
                dve.wait_ge(s_gram, t + 1)
                if t:
                    dve.wait_ge(s_flat, t)
                gram = p_gram[:, :].rearrange("p (s g) -> p g s", g=QS)
                z = zs[:, :].rearrange("p (g f) -> p g f", f=QS)
                nc.vector.transpose(z[:, 0:F, :], gram[:, 0:F, :])
                nc.vector.transpose(z[:, F:ZG, :], gram[:, 0:SHIFTS, :]).then_inc(s_z, 1)
                dve.wait_ge(s_l1, 2 * t + 2)
                for n in range(N1 // 2, N1):
                    i = nc.vector.tensor_scalar(h1[:, n, :], p_h1[1][:, n - N1 // 2, :], b1s[:, n : n + 1], 0.0, ALU.add, ALU.max)
                i.then_inc(s_h1b, 1)
                dve.wait_ge(s_l3, t + 1)
                nc.vector.tensor_copy(y[:, t * P : (t + 1) * P], p_h2[0:1, N2 * P : (N2 + 1) * P]).then_inc(s_y, 1)

        @block.tensor
        def _(pe):
            pe.wait_ge(s_eye, 16)
            pe.wait_ge(s_dense, 16)
            for t in range(T):
                for g, feats in enumerate(GROUPS):
                    n = NG * t + g
                    pe.wait_ge(s_rows[t][g], 16 * sum(f > 0 for f in feats))
                    if n >= 2:
                        pe.wait_ge(s_xt_dve if n % 2 else s_xt_act, n // 2)
                    for f in feats:
                        i = nc.tensor.transpose(p_tr[n % 2][:, (f - feats[0]) * P : (f - feats[0] + 1) * P], rows[:, t, f, :], eyes[:, :])
                    i.then_inc(s_tr, 1)
                n = NG * (t + 1)
                pe.wait_ge(s_xt_act, (n + 1) // 2)
                pe.wait_ge(s_xt_dve, n // 2)
                if t:
                    pe.wait_ge(s_z, t)
                else:
                    pe.wait_ge(s_clear, 1)
                for s in range(SLOTS):
                    for q in range(4):
                        x = xt[:, t, q * SLOTS + s, :]
                        i = nc.tensor.matmul(p_gram[q * QS : q * QS + F, s * QS : s * QS + F], x, x, start=True, stop=True)
                i.then_inc(s_gram, 1)
                pe.wait_ge(s_flat, t + 1)
                if t:
                    pe.wait_ge(s_pairs, t)
                for c in range(PC):
                    i = nc.tensor.transpose(p_pair[0:KP, c * P : (c + 1) * P], flat[:, c * KP : (c + 1) * KP], eyes[:, :])
                i.then_inc(s_pt, 1)
                if t == 0:
                    pe.wait_ge(s_w1, 32)
                pe.wait_ge(s_pairs, t + 1)
                for n in range(N1):
                    half = n // (N1 // 2)
                    if t and n % 2 == 0:
                        pe.wait_ge(s_h1b if half else s_h1a, t)
                    for k in range(2 + PC):
                        depth = D if k < 2 else KP
                        x = xt[:, t, :, 0] if k < 2 else pairs[:, k - 2, :]
                        i = nc.tensor.matmul(p_h1[half][:, n % 2, :], w1s[0:depth, k, n * P : (n + 1) * P], x,
                                             start=k == 0, stop=k == 1 + PC)
                    if n % 2:
                        i.then_inc(s_l1, 1)
                if t == 0:
                    pe.wait_ge(s_w2, 16)
                if t:
                    pe.wait_ge(s_y, t)
                pe.wait_ge(s_h1a, t + 1)
                pe.wait_ge(s_h1b, t + 1)
                for n in range(N2):
                    for k in range(N1):
                        i = nc.tensor.matmul(p_h2[:, n * P : (n + 1) * P], w2s[:, k, n * P : (n + 1) * P], h1[:, k, :],
                                             start=k == 0, stop=k == N1 - 1)
                i.then_inc(s_l2, 1)
                pe.wait_ge(s_h2, t + 1)
                for k in range(N2):
                    i = nc.tensor.matmul(p_h2[0:1, N2 * P : (N2 + 1) * P], w3s[:, k : k + 1], h2[:, k, :],
                                         start=k == 0, stop=k == N2 - 1)
                i.then_inc(s_l3, 1)


def kernel(**inputs):
    import numpy as np
    import concourse.bacc as bacc
    from concourse.bass_utils import run_bass_kernel_spmd as run

    nc = bacc.Bacc("TRN2", target_bir_lowering=False, num_devices=1)
    arrays = {}

    def given(name, a):
        a = np.ascontiguousarray(a)
        arrays[name] = a
        return nc.dram_tensor(name, a.shape, mybir.dt.from_np(a.dtype), kind="ExternalInput").ap()

    w1 = np.asarray(inputs["W_top1"])
    order = list(range(D)) + list(range(w1.shape[0] - D, w1.shape[0])) + pair_rows()
    args = [
        given("dense", inputs["r_dense_features"]),
        given("ids_", inputs["ids"]),
        [given(f"table{i}", inputs[f"tbl_{i}"]) for i in range(NT)],
        given("w1", w1[order]),
        given("b1", np.asarray(inputs["b_top1"]).reshape(N1, P).T),
        given("w2", inputs["W_top2"]),
        given("b2", np.asarray(inputs["b_top2"]).reshape(N2, P).T),
        given("w3", np.asarray(inputs["W_top3"]).reshape(N2, P).T),
        given("eye", np.eye(P, dtype=np.float32)),
        nc.dram_tensor("out", (B, 1), mybir.dt.float32, kind="ExternalOutput").ap(),
    ]
    build(nc, *args)
    return run(nc, [arrays], core_ids=[0]).results[0]["out"]
```

```python
from contextlib import ExitStack

import concourse.bass as bass
from concourse import mybir

B = 512
D = 128
VOCAB = [1000, 12500, 1000, 12500, 1000, 1250, 12500, 12500, 125000, 12500, 12500, 12500, 1250, 1000,
         1250, 12500, 1000, 1000, 12500, 1250, 1000, 1000, 1000, 1000, 1000, 1000]
NT = len(VOCAB)
F = NT + 1
P = 128
T = B // P
QS = 32
SLOTS = P // 4
H1, H2 = 512, 256
N1, N2 = H1 // P, H2 // P

HOT = 6
HOT_ROWS = min(VOCAB)
HR = 8
HP = HOT_ROWS // HR
GROUP = 4
LATE = GROUP
E = F - LATE
NG = (F - 1 - HOT) // GROUP

HOT_TABLES = [i for i in range(NT) if VOCAB[i] == HOT_ROWS][:HOT]
TABLES = HOT_TABLES + [i for i in range(NT) if i not in HOT_TABLES]
FEATURES = [0] + [1 + i for i in TABLES]

SHIFTS = (E - 1) // 2
DUP = E
LROW = E + SHIFTS
EARLY_PAIRS = E * SHIFTS
LATE_PAIRS = LATE * E + LATE * (LATE - 1) // 2
PAIRS = EARLY_PAIRS + LATE_PAIRS
CHUNKS = [(0, P), (P, EARLY_PAIRS), (EARLY_PAIRS, PAIRS)]
PC = len(CHUNKS)
LATE_SQUARE = [(l, f) for l in (E + 2, E + 3) for f in (E, E + 1)]
LATE_REST = [(E + 1, E), (E + 3, E + 2)]


def pair_rows():
    pairs = [(f, (f + k) % E) for f in range(E) for k in range(1, SHIFTS + 1)]
    pairs += [(l, f) for l in range(E, F) for f in range(E)] + LATE_SQUARE + LATE_REST
    rows = []
    for f, g in pairs:
        lo, hi = sorted((FEATURES[f], FEATURES[g]))
        rows.append(D + lo * F - lo * (lo + 1) // 2 + hi - lo - 1)
    return rows


ITEMS = [("dense",), ("ids", 0)]
for _i in range(HOT):
    ITEMS += [("ids", _i + 1)] * (_i + 1 < HOT) + [("hot", _i)]
    ITEMS += [("group", 0, _i - HOT + NG - 1)] * (_i - HOT + NG - 1 >= 0)
ITEMS += [("group", 0, NG - 1)] + [("group", _t, _g) for _t in range(1, T) for _g in range(NG)]


def by_vector(item):
    return item[0] == "group" and item[1] > 0 and item[2] in (1, 3)


def copies(n, vector):
    return sum(by_vector(x) == vector for x in ITEMS[: n + 1])


def build(nc, dense, ids, tables, w1, b1, w2, b2, w3, eye, hot_row, out):
    fp32, bf16, fp16, i32 = mybir.dt.float32, mybir.dt.bfloat16, mybir.dt.float16, mybir.dt.int32
    ALU = mybir.AluOpType
    ACT = mybir.ActivationFunctionType

    with ExitStack() as ctx:

        def sb(name, shape, dt=fp32):
            return ctx.enter_context(nc.sbuf_tensor(name, shape, dt))

        def pb(name, shape):
            return ctx.enter_context(nc.psum_tensor(name, shape, fp32))

        def sem(name):
            return ctx.enter_context(nc.semaphore(name))

        idx = sb("idx", [P, T, NT], i32)
        dense_rows = sb("dense_rows", [P, T, D])
        rows = sb("rows", [P, T, NG * GROUP, D])
        xt = sb("xt", [D, T, P, F])
        eyes = sb("eyes", [P, P])
        eye16 = sb("eye16", [P, P], fp16)

        id16 = sb("id16", [P, T, HOT], fp16)
        hot_rows = sb("hot_rows", [HP, HR])
        idb = [sb(f"idb{i}", [HP, B], fp16) for i in range(2)]
        raw = [sb(f"raw{i}", [HP, HR * D]) for i in range(2)]
        rest = sb("rest", [HP, HR * D])
        parts = [sb(f"parts{i}", [HP, 3, HR, D], bf16) for i in range(2)]
        onehot = [sb(f"onehot{i}", [HP, HR, B], bf16) for i in range(2)]

        zs = sb("zs", [P, (LROW + LATE) * QS])
        flat = sb("flat", [P, PAIRS])
        pairs = sb("pairs", [P, PC, P])
        w1s = sb("w1s", [P, 2 + PC, H1])
        w1d = sb("w1d", [P, H1])
        w2s = sb("w2s", [P, N1, H2])
        w3s = sb("w3s", [P, N2])
        b1s = sb("b1s", [P, N1])
        b2s = sb("b2s", [P, N2])
        h1 = sb("h1", [P, N1, P])
        h2 = sb("h2", [P, N2, P])
        y = sb("y", [1, B])

        p_tr = [pb(f"p_tr{i}", [P, 512]) for i in range(2)]
        p_gram = pb("p_gram", [P, SLOTS * QS])
        p_pair = pb("p_pair", [P, 512])
        p_h1 = [pb(f"p_h1{i}", [P, 2, 2 * P]) for i in range(2)]
        p_h2 = pb("p_h2", [P, 512])
        p_late = p_pair[:, 3 * P : 4 * P]

        s_ids = sem("s_ids")
        s_dense = sem("s_dense")
        s_eye = sem("s_eye")
        s_w1 = sem("s_w1")
        s_w2 = sem("s_w2")
        s_small = sem("s_small")
        s_raw = [sem(f"s_raw{i}") for i in range(2)]
        s_rows = [[sem(f"s_rows{t}_{g}") for g in range(NG)] for t in range(T)]
        s_eye16 = sem("s_eye16")
        s_id16 = sem("s_id16")
        s_clear = sem("s_clear")
        s_w1d = sem("s_w1d")
        s_hi = sem("s_hi")
        s_rest = sem("s_rest")
        s_mid = sem("s_mid")
        s_lo = sem("s_lo")
        s_onehot = sem("s_onehot")
        s_tr = sem("s_tr")
        s_act = sem("s_act")
        s_dve = sem("s_dve")
        s_gram = sem("s_gram")
        s_late = sem("s_late")
        s_ze = sem("s_ze")
        s_zl = sem("s_zl")
        s_fe = sem("s_fe")
        s_fl = sem("s_fl")
        s_fr = sem("s_fr")
        s_pt = sem("s_pt")
        s_pairs = sem("s_pairs")
        s_l1 = sem("s_l1")
        s_h1a = sem("s_h1a")
        s_h1b = sem("s_h1b")
        s_l2 = sem("s_l2")
        s_h2 = sem("s_h2")
        s_l3 = sem("s_l3")
        s_y = sem("s_y")
        s_out = sem("s_out")

        block = ctx.enter_context(nc.Block())

        @block.sync
        def _(sp):
            def load_hot(i):
                sp.dma_start(raw[i % 2][:, :], tables[TABLES[i]].rearrange("(p k) d -> p (k d)", k=HR)).then_inc(s_raw[i % 2], 16)

            sp.dma_start(idx[:, :, :], ids.rearrange("(t p) f -> p t f", p=P)).then_inc(s_ids, 16)
            load_hot(0)
            sp.dma_start(dense_rows[:, :, :], dense.rearrange("(t p) d -> p t d", p=P)).then_inc(s_dense, 16)
            load_hot(1)
            sp.dma_start(w1s[:, 0:2, :], w1[0 : 2 * D, :].rearrange("(k p) n -> p k n", p=D)).then_inc(s_w1, 16)
            for c, (a, b) in enumerate(CHUNKS):
                sp.dma_start(w1s[0 : b - a, 2 + c, :], w1[2 * D + a : 2 * D + b, :]).then_inc(s_w1, 16)
            sp.dma_start(w2s[:, :, :], w2.rearrange("(k p) n -> p k n", p=P)).then_inc(s_w2, 16)
            for i in range(2, HOT):
                sp.wait_ge(s_hi, i - 1)
                sp.wait_ge(s_rest, i - 1)
                load_hot(i)
            sp.wait_ge(s_y, T)
            sp.dma_start(out.rearrange("b o -> o b"), y[:, :]).then_inc(s_out, 16)
            sp.wait_ge(s_out, 16)

        @block.gpsimd
        def _(pool):
            pool.wait_ge(s_ids, 16)
            for t in range(T):
                for g in range(NG):
                    for j in range(g * GROUP, (g + 1) * GROUP):
                        pool.indirect_dma_start(
                            rows[:, t, j, :], None, tables[TABLES[HOT + j]],
                            bass.IndirectOffsetOnAxis(ap=idx[:, t, HOT + j : HOT + j + 1], axis=0),
                        ).then_inc(s_rows[t][g], 16)

        def copy_out(copy, n):
            kind, *which = ITEMS[n]
            bank = p_tr[n % 2]
            if kind == "ids":
                return copy(idb[which[0] % 2][:, :], bank[0:HP, :])
            if kind == "group":
                t, g = which
                f = 1 + HOT + g * GROUP
                dst = xt[:, t, :, f : f + GROUP].rearrange("d b f -> d f b")
                return copy(dst, bank[:, :].rearrange("d (f b) -> d f b", f=GROUP))
            f = 1 + which[0] if which else 0
            return copy(xt[:, :, :, f], bank[:, :].rearrange("d (t b) -> d t b", t=T))

        def pick_early(act, t):
            act.wait_ge(s_ze, t + 1)
            if t:
                act.wait_ge(s_pt, t)
            z = zs[:, :]
            z = bass.AP(z.tensor, z.offset + QS, [z.ap[0], [QS + 1, E], [QS, SHIFTS]])
            nc.scalar.copy(flat[:, 0:EARLY_PAIRS].rearrange("p (f k) -> p f k", f=E), z).then_inc(s_fe, 1)

        @block.scalar
        def _(act):
            act.dma_start(eyes[:, :], eye).then_inc(s_eye, 16)
            for dst, src in ((hot_rows, hot_row), (w3s, w3), (b1s, b1), (b2s, b2)):
                act.dma_start(dst[:, :], src).then_inc(s_small, 16)

            def first_part(i):
                act.wait_ge(s_raw[i % 2], 16 * (i // 2 + 1))
                if i >= 2:
                    act.wait_ge(s_tr, ITEMS.index(("hot", i - 2)) + 1)
                nc.scalar.copy(parts[i % 2][:, 0, :, :].rearrange("p k d -> p (k d)"), raw[i % 2][:, :]).then_inc(s_hi, 1)

            def ids_out(i):
                n = ITEMS.index(("ids", i))
                act.wait_ge(s_tr, n + 1)
                if i >= 2:
                    act.wait_ge(s_onehot, HR * (i - 1))
                copy_out(nc.scalar.copy, n).then_inc(s_act, 1)

            def second_part(i):
                act.wait_ge(s_rest, i + 1)
                nc.scalar.copy(parts[i % 2][:, 1, :, :].rearrange("p k d -> p (k d)"), rest[:, :]).then_inc(s_mid, 1)

            act.wait_ge(s_ids, 16)
            nc.scalar.copy(id16[:, :, :], idx[:, :, 0:HOT]).then_inc(s_id16, 1)
            first_part(0)
            act.wait_ge(s_tr, 1)
            copy_out(nc.scalar.copy, 0).then_inc(s_act, 1)
            ids_out(0)
            second_part(0)
            def copy_here(item):
                n = ITEMS.index(item)
                if not by_vector(item):
                    act.wait_ge(s_tr, n + 1)
                    copy_out(nc.scalar.copy, n).then_inc(s_act, 1)

            for i in range(HOT):
                if i + 1 < HOT:
                    first_part(i + 1)
                    ids_out(i + 1)
                    second_part(i + 1)
                copy_here(("hot", i))
                if i - HOT + NG - 1 >= 0:
                    copy_here(("group", 0, i - HOT + NG - 1))
            copy_here(("group", 0, NG - 1))

            act.wait_ge(s_small, 64)
            for t in range(T):
                if t < T - 1:
                    copy_here(("group", t + 1, 0))
                    copy_here(("group", t + 1, 1))
                pick_early(act, t)
                if t == T - 1:
                    copy_here(("group", t, NG - 1))
                act.wait_ge(s_zl, t + 1)
                z = zs[:, LROW * QS :].rearrange("p (l f) -> p l f", f=QS)[:, :, 0:E]
                nc.scalar.copy(flat[:, EARLY_PAIRS : EARLY_PAIRS + LATE * E].rearrange("p (l f) -> p l f", f=E), z).then_inc(s_fl, 1)
                act.wait_ge(s_pt, t + 1)
                if t:
                    act.wait_ge(s_l1, 2 * t)
                nc.scalar.copy(pairs[:, :, :], p_pair[:, 0 : PC * P].rearrange("p (c b) -> p c b", c=PC)).then_inc(s_pairs, 1)
                if t < T - 1:
                    copy_here(("group", t + 1, 2))
                act.wait_ge(s_l1, 2 * t + 1)
                if t:
                    act.wait_ge(s_l2, t)
                for n in range(N1 // 2):
                    i = nc.scalar.activation(h1[:, n, :], p_h1[0][:, n, 0:P], ACT.Relu, bias=b1s[:, n : n + 1])
                i.then_inc(s_h1a, 1)
                if t < T - 1:
                    copy_here(("group", t + 1, 3))
                act.wait_ge(s_l2, t + 1)
                for n in range(N2):
                    i = nc.scalar.activation(h2[:, n, :], p_h2[:, n * P : (n + 1) * P], ACT.Relu, bias=b2s[:, n : n + 1])
                i.then_inc(s_h2, 1)
                if t < T - 2:
                    copy_here(("group", t + 1, 4))

        @block.vector
        def _(dve):
            dve.wait_ge(s_eye, 16)
            nc.vector.tensor_copy(eye16[:, :], eyes[:, :]).then_inc(s_eye16, 1)
            dve.wait_ge(s_small, 64)
            for i in range(HOT):
                dve.wait_ge(s_hi, i + 1)
                if i:
                    dve.wait_ge(s_mid, i)
                    dve.wait_ge(s_lo, i)
                first = parts[i % 2][:, 0, :, :].rearrange("p k d -> p (k d)")
                nc.vector.tensor_sub(rest[:, :], raw[i % 2][:, :], first).then_inc(s_rest, 1)
                dve.wait_ge(s_act, copies(ITEMS.index(("ids", i)), False))
                if i >= 2:
                    dve.wait_ge(s_tr, ITEMS.index(("hot", i - 2)) + 1)
                for k in range(HR):
                    nc.vector.tensor_scalar(onehot[i % 2][:, k, :], idb[i % 2][:, :], hot_rows[:, k : k + 1], None,
                                            ALU.is_equal).then_inc(s_onehot, 1)
                dve.wait_ge(s_mid, i + 1)
                dve.wait_ge(s_rest, i + 1)
                second, third = (parts[i % 2][:, j, :, :].rearrange("p k d -> p (k d)") for j in (1, 2))
                nc.vector.tensor_sub(third, rest[:, :], second).then_inc(s_lo, 1)
            nc.vector.memset(p_gram[:, :], 0.0).then_inc(s_clear, 1)
            nc.vector.memset(p_pair[:, :], 0.0).then_inc(s_clear, 1)
            dve.wait_ge(s_w1, 16 * (1 + PC))
            nc.vector.tensor_add(w1d[:, :], w1s[:, 0, :], w1s[:, 1, :]).then_inc(s_w1d, 1)

            z = zs[:, :].rearrange("p (g f) -> p g f", f=QS)
            gram = p_gram[:, :].rearrange("p (s g) -> p g s", g=QS)

            def early(t):
                dve.wait_ge(s_gram, t + 1)
                if t:
                    dve.wait_ge(s_fe, t)
                    dve.wait_ge(s_fl, t)
                    dve.wait_ge(s_fr, t)
                nc.vector.transpose(z[:, 0:DUP, :], gram[:, 0:E, :])
                nc.vector.transpose(z[:, DUP:LROW, :], gram[:, 0:SHIFTS, :]).then_inc(s_ze, 1)

            def copy_here(item):
                n = ITEMS.index(item)
                if by_vector(item):
                    dve.wait_ge(s_tr, n + 1)
                    copy_out(nc.vector.tensor_copy, n).then_inc(s_dve, 1)

            for t in range(T):
                early(t)
                if t < T - 1:
                    nc.vector.transpose(z[:, LROW:, :], gram[:, E:F, :]).then_inc(s_zl, 1)
                else:
                    dve.wait_ge(s_late, 1)
                    nc.vector.transpose(z[:, LROW:, :], p_late.rearrange("p (s l) -> p l s", l=LATE)).then_inc(s_zl, 1)
                dve.wait_ge(s_zl, t + 1)
                if t:
                    dve.wait_ge(s_pt, t)
                at = EARLY_PAIRS + LATE * E
                nc.vector.tensor_copy(flat[:, at : at + 4].rearrange("p (l f) -> p l f", f=2), z[:, LROW + 2 : LROW + 4, E : E + 2])
                row = zs[:, :]
                row = bass.AP(row.tensor, row.offset + (LROW + 1) * QS + E, [row.ap[0], [2 * QS + 2, 2]])
                nc.vector.tensor_copy(flat[:, at + 4 : at + 6], row).then_inc(s_fr, 1)
                if t < T - 1:
                    for g in range(3):
                        copy_here(("group", t + 1, g))
                dve.wait_ge(s_l1, 2 * t + 2)
                if t:
                    dve.wait_ge(s_l2, t)
                for n in range(N1 // 2, N1):
                    i = nc.vector.tensor_scalar(h1[:, n, :], p_h1[1][:, n - N1 // 2, 0:P], b1s[:, n : n + 1], 0.0, ALU.add, ALU.max)
                i.then_inc(s_h1b, 1)
                if t < T - 1:
                    copy_here(("group", t + 1, 3))
                dve.wait_ge(s_l3, t + 1)
                nc.vector.tensor_copy(y[:, t * P : (t + 1) * P], p_h2[0:1, N2 * P : (N2 + 1) * P]).then_inc(s_y, 1)

        @block.tensor
        def _(pe):
            def bank_free(n):
                if n >= 2:
                    vector = by_vector(ITEMS[n - 2])
                    pe.wait_ge(s_dve if vector else s_act, copies(n - 2, vector))

            def spread_ids(i):
                n = ITEMS.index(("ids", i))
                bank_free(n)
                for t in range(T):
                    col = id16[:, t, i : i + 1].to_broadcast([P, HP])
                    last = nc.tensor.matmul(p_tr[n % 2][0:HP, t * P : (t + 1) * P], col, eye16[:, :], start=True, stop=True)
                last.then_inc(s_tr, 1)

            def pick_hot(i):
                n = ITEMS.index(("hot", i))
                bank_free(n)
                for j, made in enumerate((s_hi, s_mid, s_lo)):
                    pe.wait_ge(made, i + 1)
                    for k in range(HR):
                        if j == 0:
                            pe.wait_ge(s_onehot, HR * i + k + 1)
                        last = nc.tensor.matmul(p_tr[n % 2][:, :], parts[i % 2][:, j, k, :], onehot[i % 2][:, k, :],
                                                start=j == k == 0, stop=j == 2 and k == HR - 1)
                last.then_inc(s_tr, 1)

            def turn_group(t, g):
                n = ITEMS.index(("group", t, g))
                bank_free(n)
                pe.wait_ge(s_rows[t][g], 16 * GROUP)
                for j in range(GROUP):
                    last = nc.tensor.transpose(p_tr[n % 2][:, j * P : (j + 1) * P], rows[:, t, g * GROUP + j, :], eyes[:, :])
                last.then_inc(s_tr, 1)

            def copied(n):
                pe.wait_ge(s_act, copies(n, False))
                if copies(n, True):
                    pe.wait_ge(s_dve, copies(n, True))

            def layer1(t, k):
                depth = D if k == 0 else CHUNKS[k - 1][1] - CHUNKS[k - 1][0]
                for n in range(N1):
                    w = w1d if k == 0 else w1s[:, 1 + k, :]
                    x = xt[:, t, :, 0] if k == 0 else pairs[0:depth, k - 1, :]
                    last = nc.tensor.matmul(p_h1[n // 2][:, n % 2, 0:P], w[0:depth, n * P : (n + 1) * P], x,
                                            start=k == 0 and n % 2 == 0, stop=k == PC, skip_group_check=True)
                    if k == PC and n % 2:
                        last.then_inc(s_l1, 1)

            pe.wait_ge(s_eye, 16)
            pe.wait_ge(s_dense, 16)
            for t in range(T):
                last = nc.tensor.transpose(p_tr[0][:, t * P : (t + 1) * P], dense_rows[:, t, :], eyes[:, :])
            last.then_inc(s_tr, 1)
            pe.wait_ge(s_eye16, 1)
            pe.wait_ge(s_id16, 1)
            spread_ids(0)
            for i in range(HOT):
                if i + 1 < HOT:
                    spread_ids(i + 1)
                pick_hot(i)
                if i - HOT + NG - 1 >= 0:
                    turn_group(0, i - HOT + NG - 1)
            turn_group(0, NG - 1)

            def gram_tile(t, size):
                if t:
                    pe.wait_ge(s_ze, t)
                    pe.wait_ge(s_zl, t)
                else:
                    pe.wait_ge(s_clear, 2)
                for s in range(SLOTS):
                    for q in range(4):
                        x = xt[:, t, q * SLOTS + s, 0:size]
                        last = nc.tensor.matmul(p_gram[q * QS : q * QS + size, s * QS : s * QS + size], x, x, start=True, stop=True)
                last.then_inc(s_gram, 1)

            def gram_late(t):
                for s in range(SLOTS):
                    for q in range(4):
                        x = xt[:, t, q * SLOTS + s, :]
                        last = nc.tensor.matmul(p_late[q * QS : q * QS + F, s * LATE : (s + 1) * LATE], x, x[:, E:F], start=True, stop=True)
                last.then_inc(s_late, 1)

            def turn_pairs(t):
                if t:
                    pe.wait_ge(s_pairs, t)
                pe.wait_ge(s_fe, t + 1)
                pe.wait_ge(s_fl, t + 1)
                pe.wait_ge(s_fr, t + 1)
                for c, (a, b) in enumerate(CHUNKS):
                    last = nc.tensor.transpose(p_pair[0 : b - a, c * P : (c + 1) * P], flat[:, a:b], eyes[:, :])
                last.then_inc(s_pt, 1)

            def layer2(t):
                if t == 0:
                    pe.wait_ge(s_w2, 16)
                else:
                    pe.wait_ge(s_y, t)
                pe.wait_ge(s_h1a, t + 1)
                pe.wait_ge(s_h1b, t + 1)
                for n in range(N2):
                    for k in range(N1):
                        last = nc.tensor.matmul(p_h2[:, n * P : (n + 1) * P], w2s[:, k, n * P : (n + 1) * P], h1[:, k, :],
                                                start=k == 0, stop=k == N1 - 1)
                last.then_inc(s_l2, 1)

            def layer3(t):
                pe.wait_ge(s_h2, t + 1)
                for k in range(N2):
                    last = nc.tensor.matmul(p_h2[0:1, N2 * P : (N2 + 1) * P], w3s[:, k : k + 1], h2[:, k, :],
                                            start=k == 0, stop=k == N2 - 1)
                last.then_inc(s_l3, 1)

            def dense_layer1(t):
                if t == 0:
                    pe.wait_ge(s_w1d, 1)
                else:
                    pe.wait_ge(s_h1a, t)
                    pe.wait_ge(s_h1b, t)
                layer1(t, 0)

            for t in range(T - 1):
                copied(ITEMS.index(("group", t, NG - 1)))
                gram_tile(t, F)
                dense_layer1(t)
                turn_group(t + 1, 0)
                turn_group(t + 1, 1)
                turn_pairs(t)
                turn_group(t + 1, 2)
                pe.wait_ge(s_pairs, t + 1)
                for k in range(1, 1 + PC):
                    layer1(t, k)
                turn_group(t + 1, 3)
                layer2(t)
                if t + 1 < T - 1:
                    turn_group(t + 1, 4)
                layer3(t)

            t = T - 1
            dense_layer1(t)
            copied(ITEMS.index(("group", t, NG - 2)))
            gram_tile(t, E)
            pe.wait_ge(s_pairs, t)
            turn_group(t, NG - 1)
            copied(len(ITEMS) - 1)
            gram_late(t)
            pe.wait_ge(s_zl, T)
            turn_pairs(t)
            pe.wait_ge(s_pairs, t + 1)
            for k in range(1, 1 + PC):
                layer1(t, k)
            layer2(t)
            layer3(t)


def kernel(**inputs):
    import numpy as np
    import concourse.bacc as bacc
    from concourse.bass_utils import run_bass_kernel_spmd as run

    nc = bacc.Bacc("TRN2", target_bir_lowering=False, num_devices=1)
    arrays = {}

    def given(name, a):
        a = np.ascontiguousarray(a)
        arrays[name] = a
        return nc.dram_tensor(name, a.shape, mybir.dt.from_np(a.dtype), kind="ExternalInput").ap()

    w1 = np.asarray(inputs["W_top1"])
    order = list(range(D)) + list(range(w1.shape[0] - D, w1.shape[0])) + pair_rows()
    args = [
        given("dense", inputs["r_dense_features"]),
        given("ids_", np.asarray(inputs["ids"])[:, TABLES]),
        [given(f"table{i}", inputs[f"tbl_{i}"]) for i in range(NT)],
        given("w1", w1[order]),
        given("b1", np.asarray(inputs["b_top1"]).reshape(N1, P).T),
        given("w2", inputs["W_top2"]),
        given("b2", np.asarray(inputs["b_top2"]).reshape(N2, P).T),
        given("w3", np.asarray(inputs["W_top3"]).reshape(N2, P).T),
        given("eye", np.eye(P, dtype=np.float32)),
        given("hot_row", np.arange(HOT_ROWS, dtype=np.float32).reshape(HP, HR)),
        nc.dram_tensor("out", (B, 1), mybir.dt.float32, kind="ExternalOutput").ap(),
    ]
    build(nc, *args)
    return run(nc, [arrays], core_ids=[0]).results[0]["out"]
```

```python
from contextlib import ExitStack

import concourse.bass as bass
from concourse import mybir

B = 512
D = 128
VOCAB = [1000, 12500, 1000, 12500, 1000, 1250, 12500, 12500, 125000, 12500, 12500, 12500, 1250, 1000,
         1250, 12500, 1000, 1000, 12500, 1250, 1000, 1000, 1000, 1000, 1000, 1000]
NT = len(VOCAB)
F = NT + 1
P = 128
T = B // P
QS = 32
SLOTS = P // 4
H1, H2 = 512, 256
N1, N2 = H1 // P, H2 // P

WARM = 12
HOT_FROM = [0, 0, 0, 0, 0, 0, 0, 3]
HOT = len(HOT_FROM)
HOT_ROWS = min(VOCAB)
HR = 8
HP = HOT_ROWS // HR
HALVES = [slice(0, HR // 2), slice(HR // 2, HR)]

HOT_TABLES = [i for i in range(NT) if VOCAB[i] == HOT_ROWS][:HOT]
TABLES = HOT_TABLES + [i for i in range(NT) if i not in HOT_TABLES]
FEATURES = [0] + [1 + i for i in TABLES]

NG = 6
FIRST_GATHERED = [sum(t >= start for start in HOT_FROM) for t in range(T)]
STARTS = [[first, first + 4, first + 8, first + 12, first + 16, NT - 1, NT] for first in FIRST_GATHERED]
GROUPS = [[range(starts[g], starts[g + 1]) for g in range(NG)] for starts in STARTS]

SHIFTS = (F - 1) // 2
ZROWS = F + SHIFTS
PAIRS = F * SHIFTS
PC = 3
KP = PAIRS // PC
PF = F // PC

WHOLE = [(0, F, 0), (F, ZROWS, 0)]
SECOND_END = 2 * PF + SHIFTS
PIECES = [(0, PF, 0), (PF + 1, F, PF + 1), (F, SECOND_END, 0), (SECOND_END, ZROWS, SECOND_END - F)]
PIECES_READ = [1, 3, 4]

TURNS = [1, 2, 3, 3, 4, 5]
AFTER_HOT = [[("dense",)] * (_i == 0) + [("group", 0, _g) for _g in range(NG) if TURNS[_g] == _i] for _i in range(HOT)]
ITEMS = []
for _i in range(HOT):
    ITEMS += [("hot", _i)] + AFTER_HOT[_i]
ITEMS += [("group", _t, _g) for _t in range(1, T) for _g in range(NG)]

BANKS, _turned = [], 0
for _item in ITEMS:
    BANKS.append(2 + _item[1] % 2 if _item[0] == "hot" else _turned % 2)
    _turned += _item[0] != "hot"

FILL = [[(0,), (1,), (2, 3), (4,), (), (), (5,)]] + [[(), (0,), (1, 2), (3,), (), (), (4, 5)]] * (T - 3)
FILL += [[(), (0,), (1, 2), (), (3,), (4, 5), ()], [()] * 7]
BY_VECTOR = [(), (2, 3, 5)] + [(1, 2, 5)] * (T - 2)

EYE, HOT_ROW, W3, B1, B2 = 0, P, P + HR, P + HR + N2, P + HR + N2 + N1
PACKED = B2 + N2


def by_vector(item):
    return item[0] == "group" and item[2] in BY_VECTOR[item[1]]


def hot_columns(i):
    return slice(HOT_FROM[i] * P, B)


def copies(n, vector):
    return sum(by_vector(x) == vector for x in ITEMS[: n + 1])


def hot_done(i):
    return ITEMS.index(("hot", i)) + 1


def zs_done(t, c):
    if t < T - 1:
        return len(WHOLE) * (t + 1)
    return len(WHOLE) * t + PIECES_READ[c]


def pair_rows():
    rows = []
    for f in range(F):
        for k in range(1, SHIFTS + 1):
            lo, hi = sorted((FEATURES[f], FEATURES[(f + k) % F]))
            rows.append(D + lo * F - lo * (lo + 1) // 2 + hi - lo - 1)
    return rows


def build(nc, dense, ids, hot_ids, tables, w1, w2, packed, out):
    fp32, bf16, fp16, i32 = mybir.dt.float32, mybir.dt.bfloat16, mybir.dt.float16, mybir.dt.int32
    ALU = mybir.AluOpType
    ACT = mybir.ActivationFunctionType

    with ExitStack() as ctx:

        def sb(name, shape, dt=fp32):
            return ctx.enter_context(nc.sbuf_tensor(name, shape, dt))

        def pb(name, shape):
            return ctx.enter_context(nc.psum_tensor(name, shape, fp32))

        def sem(name):
            return ctx.enter_context(nc.semaphore(name))

        idx = sb("idx", [P, T, NT], i32)
        dense_rows = sb("dense_rows", [P, T, D])
        rows = sb("rows", [P, T, NT - FIRST_GATHERED[0], D])
        xt = sb("xt", [D, T, P, F])

        small = sb("small", [P, PACKED])
        eye = small[:, EYE : EYE + P]
        hot_row = small[0:HP, HOT_ROW : HOT_ROW + HR]
        w3s = small[:, W3 : W3 + N2]
        b1s = small[:, B1 : B1 + N1]
        b2s = small[:, B2 : B2 + N2]

        ids32 = [sb(f"ids32{i}", [HP, B], i32) for i in range(2)]
        idb = [sb(f"idb{i}", [HP, B], fp16) for i in range(2)]
        raw = [sb(f"raw{i}", [HP, HR, D]) for i in range(2)]
        rest = sb("rest", [HP, HR, D])
        parts = [sb(f"parts{i}", [HP, 3, HR, D], bf16) for i in range(2)]
        onehot = [sb(f"onehot{i}", [HP, HR, B], bf16) for i in range(2)]

        idle = sb("idle", [P, 512], bf16)
        zs = sb("zs", [P, ZROWS * QS])
        flat = sb("flat", [P, PAIRS])
        pairs = sb("pairs", [KP, PC, P])
        w1s = sb("w1s", [P, 2 + PC, H1])
        w1d = sb("w1d", [P, H1])
        w2s = sb("w2s", [P, N1, H2])
        h1 = sb("h1", [P, N1, P])
        h2 = sb("h2", [P, N2, P])
        y = sb("y", [1, B])

        p_tr = [pb(f"p_tr{i}", [P, 512]) for i in range(2)]
        p_gram = pb("p_gram", [P, SLOTS * QS])
        p_pair = pb("p_pair", [P, 512])
        p_h1 = [pb(f"p_h1{i}", [P, 512]) for i in range(2)]
        p_h2 = pb("p_h2", [P, 512])
        p_h2s = [p_h2[:, 0:P], p_pair[:, 3 * P : 4 * P]]
        p_items = p_tr + p_h1
        p_last_pairs = [p_pair, p_tr[0], p_tr[1]]

        s_ids = sem("s_ids")
        s_hot_ids = [sem(f"s_hot_ids{i}") for i in range(2)]
        s_dense = sem("s_dense")
        s_small = sem("s_small")
        s_w1 = sem("s_w1")
        s_w2 = sem("s_w2")
        s_raw = [sem(f"s_raw{i}") for i in range(2)]
        s_rows = [[sem(f"s_rows{t}_{g}") for g in range(NG)] for t in range(T)]
        s_idle = sem("s_idle")
        s_clear = sem("s_clear")
        s_w1d = sem("s_w1d")
        s_idb0 = sem("s_idb0")
        s_idb = sem("s_idb")
        s_hi = sem("s_hi")
        s_rest = sem("s_rest")
        s_mid = sem("s_mid")
        s_lo = sem("s_lo")
        s_onehot = sem("s_onehot")
        s_tr = sem("s_tr")
        s_act = sem("s_act")
        s_dve = sem("s_dve")
        s_gram = sem("s_gram")
        s_zs = sem("s_zs")
        s_flat = sem("s_flat")
        s_pt = sem("s_pt")
        s_pairs = sem("s_pairs")
        s_pairs_dve = sem("s_pairs_dve")
        s_l1 = sem("s_l1")
        s_h1a = sem("s_h1a")
        s_h1b = sem("s_h1b")
        s_l2 = sem("s_l2")
        s_h2a = sem("s_h2a")
        s_h2b = sem("s_h2b")
        s_l3 = sem("s_l3")
        s_y = sem("s_y")
        s_out = sem("s_out")

        block = ctx.enter_context(nc.Block())

        @block.sync
        def _(sp):
            def load_hot(i):
                table = tables[HOT_TABLES[i]].rearrange("(p k) d -> p k d", k=HR)
                sp.dma_start(raw[i % 2][:, :, :], table).then_inc(s_raw[i % 2], 16)

            def load_ids(i):
                sp.dma_start(ids32[i % 2][:, :], hot_ids[i : i + 1, :].to_broadcast([HP, B])).then_inc(s_hot_ids[i % 2], 16)

            sp.dma_start(idx[:, :, :], ids.rearrange("(t p) f -> p t f", p=P)).then_inc(s_ids, 16)
            load_ids(0)
            load_hot(0)
            load_ids(1)
            load_hot(1)
            sp.dma_start(dense_rows[:, :, :], dense.rearrange("(t p) d -> p t d", p=P)).then_inc(s_dense, 16)
            for i in range(2, HOT):
                if i == 2:
                    sp.wait_ge(s_idb0, 1)
                else:
                    sp.wait_ge(s_idb, i - 2)
                load_ids(i)
                sp.wait_ge(s_hi, 2 * (i - 1))
                sp.wait_ge(s_rest, 2 * (i - 1))
                load_hot(i)
                if i == 2:
                    sp.dma_start(w1s[:, 0:2, :], w1[0 : 2 * D, :].rearrange("(k p) n -> p k n", p=D)).then_inc(s_w1, 16)
                    sp.dma_start(w1s[0:KP, 2 : 2 + PC, :], w1[2 * D :, :].rearrange("(c p) n -> p c n", p=KP)).then_inc(s_w1, 16)
                    sp.dma_start(w2s[:, :, :], w2.rearrange("(k p) n -> p k n", p=P)).then_inc(s_w2, 16)
            sp.wait_ge(s_y, T)
            sp.dma_start(out.rearrange("b o -> o b"), y[:, :]).then_inc(s_out, 16)
            sp.wait_ge(s_out, 16)

        @block.gpsimd
        def _(pool):
            pool.wait_ge(s_ids, 16)
            for t in range(T):
                for g in range(NG):
                    for j in GROUPS[t][g]:
                        pool.indirect_dma_start(
                            rows[:, t, j - FIRST_GATHERED[0], :], None, tables[TABLES[j]],
                            bass.IndirectOffsetOnAxis(ap=idx[:, t, j : j + 1], axis=0),
                        ).then_inc(s_rows[t][g], 16)

        def copy_out(copy, n):
            kind, *which = ITEMS[n]
            bank = p_items[BANKS[n]]
            if kind == "group":
                t, g = which
                size, f = len(GROUPS[t][g]), 1 + GROUPS[t][g][0]
                dst = xt[:, t, :, f : f + size].rearrange("d b f -> d f b")
                return copy(dst, bank[:, 0 : size * P].rearrange("d (f b) -> d f b", f=size))
            f, t0 = (1 + which[0], HOT_FROM[which[0]]) if which else (0, 0)
            return copy(xt[:, t0:, :, f], bank[:, t0 * P :].rearrange("d (t b) -> d t b", b=P))

        @block.scalar
        def _(act):
            act.dma_start(small[:, :], packed).then_inc(s_small, 16)

            def copy_here(item):
                n = ITEMS.index(item)
                if not by_vector(item):
                    act.wait_ge(s_tr, n + 1)
                    copy_out(nc.scalar.copy, n).then_inc(s_act, 1)

            def ids_out(i):
                act.wait_ge(s_hot_ids[i % 2], 16 * (i // 2 + 1))
                if i >= 2:
                    act.wait_ge(s_onehot, HR * (i - 1))
                nc.scalar.copy(idb[i % 2][:, hot_columns(i)], ids32[i % 2][:, hot_columns(i)]).then_inc(s_idb, 1)

            def first_part(i):
                act.wait_ge(s_raw[i % 2], 16 * (i // 2 + 1))
                if i >= 2:
                    act.wait_ge(s_tr, hot_done(i - 2))
                for half in HALVES:
                    nc.scalar.copy(parts[i % 2][:, 0, half, :], raw[i % 2][:, half, :]).then_inc(s_hi, 1)

            def second_part(i):
                for h, half in enumerate(HALVES):
                    act.wait_ge(s_rest, 2 * i + h + 1)
                    nc.scalar.copy(parts[i % 2][:, 1, half, :], rest[:, half, :]).then_inc(s_mid, 1)

            first_part(0)
            second_part(0)
            for i in range(HOT):
                if i + 1 < HOT:
                    first_part(i + 1)
                    ids_out(i + 1)
                    second_part(i + 1)
                copy_here(("hot", i))
                for item in AFTER_HOT[i]:
                    copy_here(item)

            act.wait_ge(s_small, 16)
            for t in range(T):

                def fill(step):
                    for g in FILL[t][step]:
                        copy_here(("group", t + 1, g))

                def pick(c, end):
                    z = zs[:, :]
                    shift = 1 if t == T - 1 and c == 0 else QS
                    z = bass.AP(z.tensor, z.offset + shift + c * PF * (QS + 1), [z.ap[0], [QS + 1, (end - c) * PF], [shift, SHIFTS]])
                    act.wait_ge(s_zs, zs_done(t, end - 1))
                    if t:
                        act.wait_ge(s_pt, t)
                    once = flat[:, c * KP : end * KP].rearrange("p (f k) -> p f k", k=SHIFTS)
                    nc.scalar.copy(once, z).then_inc(s_flat, 1)

                fill(0)
                fill(1)
                if t < T - 1:
                    pick(0, PC)
                    fill(2)
                    act.wait_ge(s_pt, t + 1)
                    if t:
                        act.wait_ge(s_l1, 2 * t)
                    for a, b in ((0, 1), (1, PC)):
                        turned = p_pair[0:KP, a * P : b * P].rearrange("p (c b) -> p c b", b=P)
                        nc.scalar.copy(pairs[:, a:b, :], turned).then_inc(s_pairs, 1)
                else:
                    def pairs_out(c):
                        act.wait_ge(s_pt, t + c + 1)
                        nc.scalar.copy(pairs[:, c, :], p_last_pairs[c][0:KP, 0:P]).then_inc(s_pairs, 1)

                    act.wait_ge(s_l1, 2 * t)
                    pick(0, 1)
                    pairs_out(0)
                    pick(1, 2)
                    pick(2, 3)
                    pairs_out(2)
                fill(3)
                act.wait_ge(s_l1, 2 * t + 1)
                if t:
                    act.wait_ge(s_l2, 2 * t)
                for n in range(N1 // 2):
                    nc.scalar.activation(h1[:, n, :], p_h1[0][:, n * P : (n + 1) * P], ACT.Relu,
                                         bias=b1s[:, n : n + 1]).then_inc(s_h1a, 1)
                fill(4)
                fill(5)
                act.wait_ge(s_l2, 2 * t + 1)
                if t:
                    act.wait_ge(s_l3, t)
                nc.scalar.activation(h2[:, 0, :], p_h2s[0], ACT.Relu, bias=b2s[:, 0:1]).then_inc(s_h2a, 1)
                fill(6)

        @block.vector
        def _(dve):
            nc.vector.memset(idle[:, :], 0.0).then_inc(s_idle, 1)
            dve.wait_ge(s_small, 16)

            def compare(i, ks):
                if i:
                    dve.wait_ge(s_idb, i)
                else:
                    dve.wait_ge(s_idb0, 1)
                if i >= 2:
                    dve.wait_ge(s_tr, hot_done(i - 2))
                cols = hot_columns(i)
                for k in ks:
                    nc.vector.tensor_scalar(onehot[i % 2][:, k, cols], idb[i % 2][:, cols], hot_row[:, k : k + 1], None,
                                            ALU.is_equal).then_inc(s_onehot, 1)

            def without_first(i, h):
                dve.wait_ge(s_hi, 2 * i + h + 1)
                if i:
                    dve.wait_ge(s_mid, 2 * i)
                    dve.wait_ge(s_lo, 2 * i)
                half = HALVES[h]
                nc.vector.tensor_sub(rest[:, half, :], raw[i % 2][:, half, :], parts[i % 2][:, 0, half, :]).then_inc(s_rest, 1)

            dve.wait_ge(s_hot_ids[0], 16)
            nc.vector.tensor_copy(idb[0][:, :], ids32[0][:, :]).then_inc(s_idb0, 1)
            for i in range(HOT):
                if i == HOT // 2:
                    nc.vector.memset(p_gram[:, :], 0.0).then_inc(s_clear, 1)
                    dve.wait_ge(s_w1, 32)
                    nc.vector.tensor_add(w1d[:, :], w1s[:, 0, :], w1s[:, 1, :]).then_inc(s_w1d, 1)
                if i == 0:
                    compare(i, range(HR - 2))
                    without_first(i, 0)
                    compare(i, range(HR - 2, HR))
                    without_first(i, 1)
                else:
                    without_first(i, 0)
                    without_first(i, 1)
                    compare(i, range(HR))
                for h, half in enumerate(HALVES):
                    dve.wait_ge(s_mid, 2 * i + h + 1)
                    dve.wait_ge(s_rest, 2 * i + h + 1)
                    nc.vector.tensor_sub(parts[i % 2][:, 2, half, :], rest[:, half, :], parts[i % 2][:, 1, half, :]).then_inc(s_lo, 1)

            def results_out(t):
                row = y[:, t * P : (t + 1) * P].rearrange("o (s q) -> o q s", q=4)
                dve.wait_ge(s_l3, t + 1)
                nc.vector.tensor_copy(row, p_h2[0:1, N2 * P : (N2 + 1) * P].rearrange("o (q s) -> o q s", q=4)).then_inc(s_y, 1)

            for t in range(T):

                def fill(step):
                    for g in FILL[t][step]:
                        item = ("group", t + 1, g)
                        n = ITEMS.index(item)
                        if by_vector(item):
                            dve.wait_ge(s_tr, n + 1)
                            copy_out(nc.vector.tensor_copy, n).then_inc(s_dve, 1)

                z = zs[:, :].rearrange("p (g f) -> p g f", f=QS)
                gram = p_gram[:, :].rearrange("p (s g) -> p g s", g=QS)
                dve.wait_ge(s_gram, t + 1)
                if t:
                    dve.wait_ge(s_flat, t)
                for a, b, g in WHOLE if t < T - 1 else PIECES:
                    nc.vector.transpose(z[:, a:b, :], gram[:, g : g + b - a, :]).then_inc(s_zs, 1)
                if t == T - 1:
                    dve.wait_ge(s_pt, t + 2)
                    dve.wait_ge(s_l1, 2 * t)
                    nc.vector.tensor_copy(pairs[:, 1, :], p_last_pairs[1][0:KP, 0:P]).then_inc(s_pairs_dve, 1)
                    results_out(t - 1)
                for step in (0, 1, 2, 3):
                    fill(step)
                dve.wait_ge(s_l1, 2 * t + 2)
                if t:
                    dve.wait_ge(s_l2, 2 * t)
                for n in range(N1 // 2, N1):
                    nc.vector.tensor_scalar(h1[:, n, :], p_h1[1][:, (n - 2) * P : (n - 1) * P], b1s[:, n : n + 1], 0.0,
                                            ALU.add, ALU.max).then_inc(s_h1b, 1)
                fill(4)
                fill(5)
                dve.wait_ge(s_l2, 2 * t + 2)
                if t:
                    dve.wait_ge(s_l3, t)
                nc.vector.tensor_scalar(h2[:, 1, :], p_h2s[1], b2s[:, 1:2], 0.0, ALU.add, ALU.max).then_inc(s_h2b, 1)
                fill(6)
                if t < T - 2:
                    results_out(t)
            results_out(T - 1)

        @block.tensor
        def _(pe):
            def bank_free(n):
                if BANKS[n] in BANKS[:n]:
                    last = max(m for m in range(n) if BANKS[m] == BANKS[n])
                    vector = by_vector(ITEMS[last])
                    pe.wait_ge(s_dve if vector else s_act, copies(last, vector))

            def features_copied(t):
                n = max(ITEMS.index(("group", t, NG - 1)), *(ITEMS.index(("hot", i)) for i in range(HOT) if HOT_FROM[i] <= t))
                pe.wait_ge(s_act, copies(n, False))
                if copies(n, True):
                    pe.wait_ge(s_dve, copies(n, True))

            def pick_hot(i):
                n = ITEMS.index(("hot", i))
                cols = hot_columns(i)
                bank_free(n)
                for j, made in enumerate((s_hi, s_mid, s_lo)):
                    for k in range(HR):
                        if k % (HR // 2) == 0:
                            pe.wait_ge(made, 2 * i + 1 + k // (HR // 2))
                        if j == 0:
                            pe.wait_ge(s_onehot, HR * i + k + 1)
                        last = nc.tensor.matmul(p_items[BANKS[n]][:, cols], parts[i % 2][:, j, k, :], onehot[i % 2][:, k, cols],
                                                start=j == k == 0, stop=j == 2 and k == HR - 1)
                last.then_inc(s_tr, 1)

            def turn_dense():
                pe.wait_ge(s_dense, 16)
                for t in range(T):
                    last = nc.tensor.transpose(p_tr[0][:, t * P : (t + 1) * P], dense_rows[:, t, :], eye)
                last.then_inc(s_tr, 1)

            def turn_group(t, g):
                n = ITEMS.index(("group", t, g))
                bank_free(n)
                pe.wait_ge(s_rows[t][g], 16 * len(GROUPS[t][g]))
                for m, j in enumerate(GROUPS[t][g]):
                    last = nc.tensor.transpose(p_items[BANKS[n]][:, m * P : (m + 1) * P], rows[:, t, j - FIRST_GATHERED[0], :], eye)
                last.then_inc(s_tr, 1)

            def layer1(t, k, outputs=range(N1)):
                for n in outputs:
                    if k == 0:
                        w, x = w1d[:, n * P : (n + 1) * P], xt[:, t, :, 0].rearrange("d (s q) -> d q s", q=4)
                    else:
                        w, x = w1s[0:KP, 1 + k, n * P : (n + 1) * P], pairs[:, k - 1, :]
                    last = nc.tensor.matmul(p_h1[n // 2][:, n % 2 * P : (n % 2 + 1) * P], w, x, start=k == 0 and n % 2 == 0, stop=k == PC,
                                            skip_group_check=True)
                    if k == PC and n % 2:
                        last.then_inc(s_l1, 1)

            pe.wait_ge(s_idle, 1)
            for _ in range(WARM):
                nc.tensor.matmul(p_h1[0][:, :], idle[:, 0:P], idle[:, :], start=True, stop=True)
            pe.wait_ge(s_small, 16)
            for i in range(HOT):
                pick_hot(i)
                for kind, *which in AFTER_HOT[i]:
                    if kind == "dense":
                        turn_dense()
                    else:
                        turn_group(*which)

            def turn_pairs(c, bank):
                return nc.tensor.transpose(bank[0:KP, :], flat[:, c * KP : (c + 1) * KP], eye)

            def layer3(t):
                for k, made in enumerate((s_h2a, s_h2b)):
                    pe.wait_ge(made, t + 1)
                    last = nc.tensor.matmul(p_h2[0:1, N2 * P : (N2 + 1) * P], w3s[:, k : k + 1], h2[:, k, :],
                                            start=k == 0, stop=k == N2 - 1)
                last.then_inc(s_l3, 1)

            for t in range(T):

                def fill(step):
                    for g in FILL[t][step]:
                        turn_group(t + 1, g)

                fill(0)
                features_copied(t)
                if t:
                    pe.wait_ge(s_zs, zs_done(t - 1, PC - 1))
                else:
                    pe.wait_ge(s_clear, 1)
                for s in range(SLOTS):
                    for q in range(4):
                        x = xt[:, t, 4 * s + q, :]
                        last = nc.tensor.matmul(p_gram[q * QS : q * QS + F, s * QS : s * QS + F], x, x, start=True, stop=True)
                last.then_inc(s_gram, 1)
                if t:
                    pe.wait_ge(s_h1a, 2 * t)
                    pe.wait_ge(s_h1b, 2 * t)
                else:
                    pe.wait_ge(s_w1d, 1)
                    pe.wait_ge(s_act, copies(ITEMS.index(("hot", HOT - 1)), False))
                fill(1)
                layer1(t, 0)
                fill(2)

                if t:
                    pe.wait_ge(s_pairs, 2 * t)
                pe.wait_ge(s_flat, t + 1)
                if t < T - 1:
                    for c in range(PC):
                        last = turn_pairs(c, p_pair[:, c * P : (c + 1) * P])
                    last.then_inc(s_pt, 1)
                    fill(3)
                    pe.wait_ge(s_pairs, 2 * t + 1)
                    layer1(t, 1)
                    pe.wait_ge(s_pairs, 2 * t + 2)
                else:
                    turn_pairs(0, p_last_pairs[0][:, 0:P]).then_inc(s_pt, 1)
                    layer3(t - 1)
                    pe.wait_ge(s_pairs, 2 * t + 1)
                    layer1(t, 1, [0])
                    pe.wait_ge(s_flat, t + 2)
                    turn_pairs(1, p_last_pairs[1][:, 0:P]).then_inc(s_pt, 1)
                    layer1(t, 1, [1])
                    pe.wait_ge(s_flat, t + 3)
                    turn_pairs(2, p_last_pairs[2][:, 0:P]).then_inc(s_pt, 1)
                    layer1(t, 1, range(2, N1))
                for n in range(N1):
                    for c in range(1, PC):
                        if t == T - 1 and n == 0:
                            if c == 1:
                                pe.wait_ge(s_pairs_dve, 1)
                            else:
                                pe.wait_ge(s_pairs, 2 * t + c)
                        layer1(t, 1 + c, [n])
                fill(4)

                if t == 0:
                    pe.wait_ge(s_w2, 16)
                else:
                    pe.wait_ge(s_y, t)

                def layer2(k, n):
                    return nc.tensor.matmul(p_h2s[n], w2s[:, k, n * P : (n + 1) * P], h1[:, k, :], start=k == 0, stop=k == N1 - 1)

                for k in range(N1 // 2):
                    pe.wait_ge(s_h1a, 2 * t + k + 1)
                    for n in range(N2):
                        layer2(k, n)
                fill(5)
                for n in range(N2):
                    for k in range(N1 // 2, N1):
                        if n == 0:
                            pe.wait_ge(s_h1b, 2 * t + k - 1)
                        last = layer2(k, n)
                    last.then_inc(s_l2, 1)
                fill(6)
                if t < T - 2:
                    layer3(t)
            layer3(T - 1)


def kernel(**inputs):
    import numpy as np
    import concourse.bacc as bacc
    from concourse.bass_utils import run_bass_kernel_spmd as run

    nc = bacc.Bacc("TRN2", target_bir_lowering=False, num_devices=1)
    arrays = {}

    def given(name, a):
        a = np.ascontiguousarray(a)
        arrays[name] = a
        return nc.dram_tensor(name, a.shape, mybir.dt.from_np(a.dtype), kind="ExternalInput").ap()

    w1 = np.asarray(inputs["W_top1"])
    order = list(range(D)) + list(range(w1.shape[0] - D, w1.shape[0])) + pair_rows()
    rows = np.zeros((P, HR), np.float32)
    rows[:HP] = np.arange(HOT_ROWS).reshape(HP, HR)
    by_tile = [np.asarray(inputs[x]).reshape(-1, P).T for x in ("W_top3", "b_top1", "b_top2")]
    packed = np.concatenate([np.eye(P, dtype=np.float32), rows] + by_tile, axis=1)
    args = [
        given("dense", inputs["r_dense_features"]),
        given("ids_", np.asarray(inputs["ids"])[:, TABLES]),
        given("hot_ids", np.asarray(inputs["ids"])[:, HOT_TABLES].T),
        [given(f"table{i}", inputs[f"tbl_{i}"]) for i in range(NT)],
        given("w1", w1[order]),
        given("w2", inputs["W_top2"]),
        given("packed", packed),
        nc.dram_tensor("out", (B, 1), mybir.dt.float32, kind="ExternalOutput").ap(),
    ]
    build(nc, *args)
    return run(nc, [arrays], core_ids=[0]).results[0]["out"]
```
